# Optimizing a Trainium2 kernel written in Bass

```python
import numpy as np
import jax
import jax.numpy as jnp

def _softmax(x, axis=-1):
    return jax.nn.softmax(x, axis=axis)

def _gelu(x):
    return jax.nn.gelu(x, approximate=True)

def _silu(x):
    return jax.nn.silu(x)

def _sigmoid(x):
    return jax.nn.sigmoid(x)

def _layernorm(x, axis=-1, eps=1e-05):
    m = jnp.mean(x, axis=axis, keepdims=True)
    v = jnp.var(x, axis=axis, keepdims=True)
    return (x - m) / jnp.sqrt(v + eps)

def _scatter_add(tgt, idx, src, axis=0):
    return tgt.at[idx].add(src)

def _segment_sum(src, seg, n):
    return jax.ops.segment_sum(src, seg, n)
kernel_name = 'mk_vit_tower_d1_tok_img1024_r4_ce68cd'

def setup_inputs(seed: int=0):
    np.random.seed(seed)
    _w = jnp.asarray

    def _rec_inputs():
        import jax
        import jax.numpy as jnp
        _rk = jax.random.key(seed)
        x = -0.00150118 + 0.499729 * jax.random.normal(jax.random.fold_in(_rk, 1), (16, 256, 64, 2), jnp.float32)
        return x
    x = _rec_inputs()

    def _L0_tok_setup():
        import jax, jax.numpy as jnp
        import numpy as np
        import math
        H = 256
        N = 64
        CH = 1
        SEQ_L = 256
        key = jax.random.key(seed)
        k1, k2, k3, k4 = jax.random.split(key, 4)
        log_dt = jax.random.uniform(k1, (H,), dtype=jnp.float32, minval=math.log(0.001), maxval=math.log(0.1))
        inv_A_real = jnp.log(0.5 * jnp.ones((H, N), jnp.float32)) + 0.1 * jax.random.normal(k2, (H, N), dtype=jnp.float32)
        A_imag = jnp.broadcast_to(math.pi * jnp.arange(N, dtype=jnp.float32), (H, N)).copy()
        B_ri = jax.random.normal(k3, (H, N, 2), dtype=jnp.float32) * 0.5
        C_ri = jax.random.normal(k4, (CH, H, N, 2), dtype=jnp.float32) * 0.5
        return {'log_dt': log_dt, 'inv_A_real': inv_A_real, 'A_imag': A_imag, 'B_ri': B_ri, 'C_ri': C_ri, 'L': SEQ_L}
    _L0_tok_all = _L0_tok_setup()
    _L0_tok_in = {k: v for k, v in _L0_tok_all.items() if k in ('log_dt', 'inv_A_real', 'A_imag', 'B_ri')}
    del _L0_tok_all

    def _L0_attn_setup():
        import jax, jax.numpy as jnp
        import numpy as np
        DIM = 256
        HEADS = 16
        HIDDEN = 1024
        EPS_ATTN = 1e-06
        EPS_LN = 1e-05

        def layer_norm(x, g, b):
            mu = jnp.mean(x, axis=-1, keepdims=True)
            var = jnp.var(x, axis=-1, keepdims=True)
            return (x - mu) * jax.lax.rsqrt(var + EPS_LN) * g + b
        key = jax.random.key(seed)
        ks = jax.random.split(key, 8)
        s = 0.02
        return {'x': jax.random.normal(ks[0], (4, 1024, DIM), jnp.float32), 'norm1_g': jnp.ones((DIM,), jnp.float32), 'norm1_b': jnp.zeros((DIM,), jnp.float32), 'qkv_w': jax.random.normal(ks[1], (3 * DIM, DIM), jnp.float32) * s, 'proj_w': jax.random.normal(ks[2], (DIM, DIM), jnp.float32) * s, 'proj_b': jnp.zeros((DIM,), jnp.float32), 'norm2_g': jnp.ones((DIM,), jnp.float32), 'norm2_b': jnp.zeros((DIM,), jnp.float32), 'fc1_w': jax.random.normal(ks[3], (HIDDEN, DIM), jnp.float32) * s, 'fc1_b': jnp.zeros((HIDDEN,), jnp.float32), 'fc2_w': jax.random.normal(ks[4], (DIM, HIDDEN), jnp.float32) * s, 'fc2_b': jnp.zeros((DIM,), jnp.float32)}
    _L0_attn_all = _L0_attn_setup()
    _L0_attn_in = {k: v for k, v in _L0_attn_all.items() if k in ('norm1_g', 'norm1_b', 'qkv_w', 'proj_w', 'proj_b', 'norm2_g', 'norm2_b', 'fc1_w', 'fc1_b', 'fc2_w', 'fc2_b')}
    del _L0_attn_all

    def _L0_ffn_setup():
        import jax, jax.numpy as jnp
        import numpy as np
        D_MODEL = 256
        DEPTH = 8
        M = 2 ** DEPTH
        N_INTERNAL = M - 1
        B, T = (8, 1024)

        def _leaf_probs(gate):
            BT = gate.shape[0]
            lp = jnp.ones((BT, M), dtype=gate.dtype)
            for level in range(DEPTH):
                n = 2 ** level
                half = M // (2 * n)
                g = gate[:, n - 1:2 * n - 1]
                f = jnp.stack([1.0 - g, g], axis=-1)
                f = jnp.broadcast_to(f[..., None], (BT, n, 2, half))
                lp = lp * f.reshape(BT, M)
            return lp
        key = jax.random.key(seed)
        ks = jax.random.split(key, 7)
        x = jax.random.normal(ks[0], (B, T, D_MODEL), dtype=jnp.float32)
        Wq = jax.random.normal(ks[1], (D_MODEL, D_MODEL), dtype=jnp.float32) * 0.02
        routers = jax.random.normal(ks[2], (N_INTERNAL, D_MODEL), dtype=jnp.float32) * 0.02
        leaf_keys = jax.random.normal(ks[3], (M, D_MODEL), dtype=jnp.float32) * 0.02
        leaf_values = jax.random.normal(ks[4], (M, D_MODEL), dtype=jnp.float32) * 0.02
        Wout_w = jax.random.normal(ks[5], (D_MODEL, D_MODEL), dtype=jnp.float32) * 0.02
        Wout_b = jax.random.normal(ks[6], (D_MODEL,), dtype=jnp.float32) * 0.02
        return {'x': x, 'Wq': Wq, 'routers': routers, 'leaf_keys': leaf_keys, 'leaf_values': leaf_values, 'Wout_w': Wout_w, 'Wout_b': Wout_b}
    _L0_ffn_all = _L0_ffn_setup()
    _L0_ffn_in = {k: v for k, v in _L0_ffn_all.items() if k in ('Wq', 'routers', 'leaf_keys', 'leaf_values', 'Wout_w', 'Wout_b')}
    del _L0_ffn_all
    return {'x': x, 'L0_tok_log_dt': _L0_tok_in['log_dt'], 'L0_tok_inv_A_real': _L0_tok_in['inv_A_real'], 'L0_tok_A_imag': _L0_tok_in['A_imag'], 'L0_tok_B_ri': _L0_tok_in['B_ri'], 'L0_attn_norm1_g': _L0_attn_in['norm1_g'], 'L0_attn_norm1_b': _L0_attn_in['norm1_b'], 'L0_attn_qkv_w': _L0_attn_in['qkv_w'], 'L0_attn_proj_w': _L0_attn_in['proj_w'], 'L0_attn_proj_b': _L0_attn_in['proj_b'], 'L0_attn_norm2_g': _L0_attn_in['norm2_g'], 'L0_attn_norm2_b': _L0_attn_in['norm2_b'], 'L0_attn_fc1_w': _L0_attn_in['fc1_w'], 'L0_attn_fc1_b': _L0_attn_in['fc1_b'], 'L0_attn_fc2_w': _L0_attn_in['fc2_w'], 'L0_attn_fc2_b': _L0_attn_in['fc2_b'], 'L0_ffn_Wq': _L0_ffn_in['Wq'], 'L0_ffn_routers': _L0_ffn_in['routers'], 'L0_ffn_leaf_keys': _L0_ffn_in['leaf_keys'], 'L0_ffn_leaf_values': _L0_ffn_in['leaf_values'], 'L0_ffn_Wout_w': _L0_ffn_in['Wout_w'], 'L0_ffn_Wout_b': _L0_ffn_in['Wout_b']}

def reference(x, L0_tok_log_dt, L0_tok_inv_A_real, L0_tok_A_imag, L0_tok_B_ri, L0_attn_norm1_g, L0_attn_norm1_b, L0_attn_qkv_w, L0_attn_proj_w, L0_attn_proj_b, L0_attn_norm2_g, L0_attn_norm2_b, L0_attn_fc1_w, L0_attn_fc1_b, L0_attn_fc2_w, L0_attn_fc2_b, L0_ffn_Wq, L0_ffn_routers, L0_ffn_leaf_keys, L0_ffn_leaf_values, L0_ffn_Wout_w, L0_ffn_Wout_b):
    import jax
    import jax.numpy as jnp

    def _L0_tok_ref(log_dt, inv_A_real, A_imag, B_ri, C_ri, L):
        import jax, jax.numpy as jnp
        import numpy as np
        import math
        H = 256
        N = 64
        CH = 1
        SEQ_L = 256
        dt = jnp.exp(log_dt)
        A = -jnp.exp(inv_A_real) + 1j * A_imag
        B = B_ri[..., 0] + 1j * B_ri[..., 1]
        C = C_ri[..., 0] + 1j * C_ri[..., 1]
        dtA = A * dt[:, None]
        dA = (1.0 + dtA / 2) / (1.0 - dtA / 2)
        C_term = C * B[None]
        log_dA = jnp.log(dA)
        V = jnp.exp(log_dA[:, :, None] * jnp.arange(L))
        K = 2.0 * jnp.einsum('chn,hnl->chl', C_term, V).real
        return K.astype(jnp.float32)

    def _L0_attn_ref(x, norm1_g, norm1_b, qkv_w, proj_w, proj_b, norm2_g, norm2_b, fc1_w, fc1_b, fc2_w, fc2_b):
        import jax, jax.numpy as jnp
        import numpy as np
        DIM = 256
        HEADS = 16
        HIDDEN = 1024
        EPS_ATTN = 1e-06
        EPS_LN = 1e-05

        def layer_norm(x, g, b):
            mu = jnp.mean(x, axis=-1, keepdims=True)
            var = jnp.var(x, axis=-1, keepdims=True)
            return (x - mu) * jax.lax.rsqrt(var + EPS_LN) * g + b
        B, N, C = x.shape
        H = HEADS
        d = C // H
        h = layer_norm(x, norm1_g, norm1_b)
        qkv = jnp.einsum('bnc,oc->bno', h, qkv_w)
        qkv = qkv.reshape(B, N, 3, H, d)
        q = jnp.transpose(qkv[:, :, 0], (0, 2, 1, 3))
        k = jnp.transpose(qkv[:, :, 1], (0, 2, 1, 3))
        v = jnp.transpose(qkv[:, :, 2], (0, 2, 1, 3))
        q = jax.nn.elu(q) + 1.0
        k = jax.nn.elu(k) + 1.0
        kv = jnp.einsum('bhnd,bhne->bhde', k, v)
        ksum = jnp.sum(k, axis=2)
        z = 1.0 / (jnp.einsum('bhnd,bhd->bhn', q, ksum) + EPS_ATTN)
        attn_out = jnp.einsum('bhnd,bhde->bhne', q, kv) * z[..., None]
        attn_out = jnp.transpose(attn_out, (0, 2, 1, 3)).reshape(B, N, C)
        attn_out = jnp.einsum('bnc,oc->bno', attn_out, proj_w) + proj_b
        x = x + attn_out
        h = layer_norm(x, norm2_g, norm2_b)
        h = jax.nn.gelu(jnp.einsum('bnc,hc->bnh', h, fc1_w) + fc1_b, approximate=False)
        h = jnp.einsum('bnh,ch->bnc', h, fc2_w) + fc2_b
        return x + h

    def _L0_ffn_ref(x, Wq, routers, leaf_keys, leaf_values, Wout_w, Wout_b):
        import jax, jax.numpy as jnp
        import numpy as np
        D_MODEL = 256
        DEPTH = 8
        M = 2 ** DEPTH
        N_INTERNAL = M - 1
        B, T = (8, 1024)

        def _leaf_probs(gate):
            BT = gate.shape[0]
            lp = jnp.ones((BT, M), dtype=gate.dtype)
            for level in range(DEPTH):
                n = 2 ** level
                half = M // (2 * n)
                g = gate[:, n - 1:2 * n - 1]
                f = jnp.stack([1.0 - g, g], axis=-1)
                f = jnp.broadcast_to(f[..., None], (BT, n, 2, half))
                lp = lp * f.reshape(BT, M)
            return lp
        Bv, Tv, d = x.shape
        q = jnp.einsum('btd,ed->bte', x, Wq)
        q_flat = q.reshape(Bv * Tv, d)
        gate = jax.nn.sigmoid(q_flat @ routers.T)
        leaf_prob = _leaf_probs(gate)
        ret = (leaf_prob @ leaf_values).reshape(Bv, Tv, d)
        return jnp.einsum('btd,ed->bte', ret, Wout_w) + Wout_b
    h = _L0_tok_ref(L0_tok_log_dt, L0_tok_inv_A_real, L0_tok_A_imag, L0_tok_B_ri, x, 256)
    h = h + _L0_attn_ref(_layernorm(h, axis=-1), L0_attn_norm1_g, L0_attn_norm1_b, L0_attn_qkv_w, L0_attn_proj_w, L0_attn_proj_b, L0_attn_norm2_g, L0_attn_norm2_b, L0_attn_fc1_w, L0_attn_fc1_b, L0_attn_fc2_w, L0_attn_fc2_b)
    h = h + _L0_ffn_ref(_layernorm(h, axis=-1), L0_ffn_Wq, L0_ffn_routers, L0_ffn_leaf_keys, L0_ffn_leaf_values, L0_ffn_Wout_w, L0_ffn_Wout_b)
    return h

_drawn_inputs = setup_inputs


def setup_inputs(seed=0):
    import zlib

    import numpy as np

    out = dict(_drawn_inputs(seed))
    spreads = {'L0_attn_norm1_g': (1.0, 0.6),
     'L0_attn_norm1_b': (0.0, 0.8),
     'L0_attn_proj_b': (0.0, 0.409),
     'L0_attn_norm2_g': (1.0, 0.6),
     'L0_attn_norm2_b': (0.0, 2.0),
     'L0_attn_fc1_b': (0.0, 0.8),
     'L0_attn_fc2_b': (0.0, 0.403)}
    factors = {'L0_attn_qkv_w': 8.0,
     'L0_attn_proj_w': 8.0,
     'L0_ffn_Wq': 8.0,
     'L0_ffn_routers': 8.0,
     'L0_ffn_leaf_values': 8.0,
     'L0_ffn_Wout_w': 8.0,
     'L0_ffn_Wout_b': 21.6,
     'L0_tok_inv_A_real': 2.674}
    for name, (base, spread) in spreads.items():
        noise = np.random.default_rng([zlib.crc32(name.encode()), seed]).standard_normal(out[name].shape)
        drawn = base * np.exp(spread * noise) if base else spread * noise
        out[name] = jnp.asarray(drawn.astype(out[name].dtype))
    for name, factor in factors.items():
        out[name] = (out[name] * factor).astype(out[name].dtype)
    return out
```

```python
from contextlib import ExitStack

import concourse.bass as bass
from concourse import mybir

ALU = mybir.AluOpType
ACT = mybir.ActivationFunctionType
F32 = mybir.dt.float32
F32R = mybir.dt.float32r

P = 128
B, H, N, L = 16, 256, 64, 256
D = L
KD = D // P
HALVES = H // P
EPS = 1e-5
EPS_ATTN = 1e-6

NE = 8
NA = P // NE
CH = 16
SUB = 8
CHUNKS = H // CH
PAIRS = CHUNKS // 2
LOGS = 8

HEADS, HD = 16, 16
HPB = P // HD
QW = P + HPB
HID = 1024
JH = HID // P
TT = 4
GT = TT * P
GROUPS = B * H // GT
CQ = B // TT
LEVELS = 8
LEAVES = 256

DVE_U = 17
DVE_POWERS = DVE_U + 4 * (LOGS - 1)
DVE_TABLES = DVE_POWERS + 2 + 3 * 6 + 3
DVE_BCOL = DVE_TABLES + 5
DVE_QKV = DVE_BCOL + KD
DVE_ALL = DVE_QKV + 2
DVE_ROUT = DVE_ALL + 1
DVE_FC1 = DVE_ROUT + 1 + KD
DVE_W2 = DVE_FC1 + 3 + 2 * KD
POOL_TABLES = 16

CREDIT = 64


def vit_tower(nc, logdt, inv_ar, a_im, b_ri, c_ri, n1g, n1b, qkvT, projT, proj_b, n2g, n2b, fc1T, fc1_b,
              fc2T, fc2_b, wq, routersT, leafT, woutT, wout_b, consts, out):
    with ExitStack() as ctx:
        def size(shape):
            n = 4
            for s in shape[1:]:
                n *= s
            return -(-n // 32) * 32

        cursor = [-(-nc.sbuf_base // 32) * 32]

        def sb(name, shape, dt=F32):
            t = nc.alloc_sbuf_tensor_at(name, shape, dt, offset=cursor[0])
            cursor[0] += size(shape)
            return t

        def ps(name, shape):
            return ctx.enter_context(nc.psum_tensor(name, shape, F32))

        sems = []
        paces = ctx.enter_context(nc.semaphore("paces"))

        def sem(name):
            s = ctx.enter_context(nc.semaphore(name))
            return s

        def lsem(name):
            s = sem(name)
            sems.append(s)
            return s

        h0 = sb("h0", [P, HALVES, B, D])
        mr = sb("mr", [P, 2, HALVES, B])
        kvm = sb("kvm", [P, B, KD, QW])
        const = sb("const", [P, P + P + HPB])
        ident, mask, mask8 = const[:, 0:P], const[:, P:2 * P], const[:, 2 * P:2 * P + HPB]
        ones = sb("ones", [P, P])
        halfpow = sb("halfpow", [P, TT])
        fc1bias = sb("fc1bias", [P, JH])
        qbias = sb("qbias", [P, KD])
        nrm = sb("nrm", [P, 4, KD])
        shared = cursor[0]

        Er = sb("Er", [P, H, NE])
        Ei = sb("Ei", [P, H, NE])
        X = sb("X", [P, H, NA])
        prods_at = cursor[0]
        prods = sb("prods", [P, 2, 2, SUB, P])
        after_prods = cursor[0]
        cursor[0] = prods_at
        pw = sb("pw", [P, LOGS, 2, H])
        assert cursor[0] <= after_prods
        weights_end = after_prods

        cursor[0] = shared
        projh, projl = (sb(f"proj{x}", [P, KD, D], F32R) for x in "hl")
        fc1h, fc1l = (sb(f"fc1{x}", [P, KD, HID], F32R) for x in "hl")
        fc2h, fc2l = (sb(f"fc2{x}", [P, JH, D], F32R) for x in "hl")
        gateh, gatel = (sb(f"gate{x}", [P, KD, LEAVES], F32R) for x in "hl")
        leafh, leafl = (sb(f"leaf{x}", [P, KD, D], F32R) for x in "hl")
        assert cursor[0] <= weights_end

        cursor[0] = weights_end
        setup_at = cursor[0]
        Y = sb("Y", [P, H, NE])
        tX = sb("tX", [P, H, NE])
        tE = sb("tE", [P, H, NE // 2])
        qkvraw = sb("qkvraw", [P, KD, 3 * D])
        rest_at = cursor[0]
        cursor[0] = setup_at
        fc1raw = sb("fc1raw", [P, KD, HID])
        fc2raw = sb("fc2raw", [P, JH, D])
        projraw = sb("projraw", [P, KD, D])
        wqraw = sb("wqraw", [P, KD, D])
        routraw = sb("routraw", [P, KD, LEAVES])
        leafraw = sb("leafraw", [P, KD, LEAVES])
        woutraw = sb("woutraw", [P, KD, D])
        assert cursor[0] <= rest_at

        cursor[0] = rest_at
        sgn = sb("sgn", [P, 2])
        u128 = sb("u128", [P, 2, H])
        W = sb("W", [P, 2, 2, CH, B, 2])
        craw = sb("craw", [P, 2, 2, CH, B])
        wt = sb("wt", [P, 2, CH, B])
        tokev = sb("tokev", [P, 2, CH // 4, P])
        qkvh, qkvl = (sb(f"qkv{x}", [P, KD, 3 * D], F32R) for x in "hl")
        kvbh = sb("kvbh", [N, 2 * D], F32R)
        kvb = sb("kvb", [N, 2 * D], F32R)
        onesr = sb("onesr", [N, P], F32R)
        bcol = sb("bcol", [P, KD, N])
        xh = sb("xh", [P, TT, D])
        bst1 = sb("bst1", [P, TT, 6])
        mv1 = sb("mv1", [P, TT, 2])
        pst1 = sb("pst1", [P, 7, TT])
        yh, yl = (sb(f"y{x}", [P, KD, GT], F32R) for x in "hl")
        qe = sb("qe", [P, KD, GT])
        qr = sb("qr", [P, KD, GT])
        ke = sb("ke", [P, 2, D])
        kr = sb("kr", [P, 2, D])
        kt = sb("kt", [P, 2, D])
        vt = sb("vt", [P, 2, KD, P + 1])
        kvraw = sb("kvraw", [P, B, KD, P + 1])
        kvs = sb("kvs", [P, KD, P + 1])
        phase1_end = cursor[0]
        tab_at = cursor[0]
        cursor[0] = tab_at
        cursor[0] = phase1_end - size([P, KD, P + 1]) - size([P, B, KD, P + 1])
        ldt = sb("ldt", [P, H])
        iar = sb("iar", [P, H])
        aim = sb("aim", [P, H])
        btab = sb("btab", [P, 2, H])
        base = sb("base", [P, 10, H])
        assert cursor[0] <= phase1_end

        cursor[0] = weights_end
        qf = sb("qf", [P, KD, TT, P])
        x1 = sb("x1", [P, TT, D])
        att = sb("att", [P, TT, D])
        zden = sb("zden", [P, TT * KD, HPB])
        zrec = sb("zrec", [P, TT * KD, HPB])
        aTh, aTl = (sb(f"aT{x}", [P, KD, GT], F32R) for x in "hl")
        x2 = sb("x2", [P, TT, D])
        xh2 = att
        x2Th, x2Tl = (sb(f"x2T{x}", [P, 2, KD, GT], F32R) for x in "hl")
        gf = sb("gf", [P, 2, GT])
        gh, gl = (sb(f"g{x}", [P, 2, GT], F32R) for x in "hl")
        r2 = sb("r2", [P, 2, TT, D])
        h1 = sb("h1", [P, TT, D])
        x4 = sb("x4", [P, TT, D])
        o1 = sb("o1", [P, TT, D])
        x4Th, x4Tl = (sb(f"x4T{x}", [P, KD, GT], F32R) for x in "hl")
        th = sb("th", [P, TT, LEAVES])
        lpA = sb("lpA", [P, TT, LEAVES // 2])
        lpB = sb("lpB", [P, TT, LEAVES])
        lTh, lTl = (sb(f"lT{x}", [P, KD, GT], F32R) for x in "hl")
        outb = sb("outb", [P, TT, D])
        bst2 = sb("bst2", [P, TT, 6])
        mv2 = sb("mv2", [P, TT, 2])
        pst2 = sb("pst2", [P, 2, TT])
        bst4 = sb("bst4", [P, TT, 6])
        mv4 = sb("mv4", [P, TT, 2])
        pst4 = sb("pst4", [P, 2, TT])
        pbias = sb("pbias", [P, D])
        fc2bias = sb("fc2bias", [P, D])
        woutbias = sb("woutbias", [P, D])
        assert max(cursor[0], phase1_end) <= nc.sbuf_usable_end, (cursor[0], phase1_end)

        PS = ps("PS", [P, 8, 512])
        def bank(b, w=512):
            return PS[:, b, 0:w]

        h0s = nc.dram_tensor("h0_scratch", [H, B, 2, P], F32, kind="Internal").ap()
        qs = nc.dram_tensor("q_scratch", [KD, P, HALVES, B * P], F32, kind="Internal").ap()

        ld_tab, ld_qkv, ld_const, ld_w2 = sem("ld_tab"), sem("ld_qkv"), sem("ld_const"), sem("ld_w2")
        act_tab, dve_set, pool_set, pe_set = sem("act_tab"), sem("dve_set"), sem("pool_set"), sem("pe_set")
        act_set = sem("act_set")
        cld = [lsem(f"cld{i}") for i in range(2)]
        c2done = lsem("c2done")
        wdone = lsem("wdone")
        vdone = lsem("vdone")
        tokmm = lsem("tokmm")
        tokout = lsem("tokout")
        h0st = [lsem(f"h0st{i}") for i in range(2)]
        h0ld = sem("h0ld")
        st1, r1done, xh1 = lsem("st1"), lsem("r1done"), lsem("xh1")
        yT, yhd, yld = lsem("yT"), lsem("yhd"), lsem("yld")
        qmm, qact, qdone = lsem("qmm"), lsem("qact"), lsem("qdone")
        qst = [lsem(f"qst{i}") for i in range(KD)]
        kvmm, kvact, kdone = lsem("kvmm"), lsem("kvact"), lsem("kdone")
        ksmm, ksum0, ksum1 = lsem("ksmm"), lsem("ksum0"), lsem("ksum1")
        qfd = lsem("qfd")
        attmm, attdone, attT, attTh, attTl = (lsem(x) for x in ("attmm", "attdone", "attT", "attTh", "attTl"))
        x1done, x1b = lsem("x1done"), lsem("x1b")
        prmm, x2done, v2done, xh2done = (lsem(x) for x in ("prmm", "x2done", "v2done", "xh2done"))
        x2T, x2Thd, x2Tld, r2done = (lsem(x) for x in ("x2T", "x2Thd", "x2Tld", "r2done"))
        f1mm, gact, gldone, f2mm = (lsem(x) for x in ("f1mm", "gact", "gldone", "f2mm"))
        h1done, v4done, x4done, o1done = (lsem(x) for x in ("h1done", "v4done", "x4done", "o1done"))
        x4T, x4Thd, x4Tld, gtmm = (lsem(x) for x in ("x4T", "x4Thd", "x4Tld", "gtmm"))
        thdone, tree, lT, lThd, lTld = (lsem(x) for x in ("thdone", "tree", "lT", "lThd", "lTld"))
        lvmm, outdone, outst = (lsem(x) for x in ("lvmm", "outdone", "outst"))

        block = ctx.enter_context(nc.Block())

        def apart(eng):
            eng.sem_inc(paces, 1)

        def three(pe, dst, ah, al, bh, bl, start, stop, **kw):
            pe.matmul(dst, ah, bh, start=start, stop=False, **kw)
            pe.matmul(dst, al, bh, start=False, stop=False, **kw)
            return pe.matmul(dst, ah, bl, start=False, stop=stop, **kw)

        @block.sync
        def _(sp):
            sp.dma_start(ldt[:, :], logdt.unsqueeze(0).to_broadcast([P, H])).then_inc(ld_tab, 16)
            for r in range(2):
                rows = slice(r * N, (r + 1) * N)
                sp.dma_start(iar[rows, :], inv_ar).then_inc(ld_tab, 16)
                sp.dma_start(aim[rows, :], a_im).then_inc(ld_tab, 16)
                sp.dma_start(btab[rows, 0, :], b_ri[r]).then_inc(ld_tab, 16)
                sp.dma_start(btab[rows, 1, :], b_ri[1 - r]).then_inc(ld_tab, 16)
            sp.dma_start(const[:, :], consts).then_inc(ld_const, 16)
            for n, v in enumerate((n1g, n1b, n2g, n2b)):
                sp.dma_start(nrm[:, n, :], v).then_inc(ld_const, 16)
            sp.dma_start(fc1bias[:, :], fc1_b).then_inc(ld_const, 16)
            sp.dma_start(qkvraw[:, :, :], qkvT.rearrange("(k p) o -> p k o", p=P)).then_inc(ld_qkv, 16)
            for s in sems:
                sp.sem_inc(s, CREDIT)

            def load_c(it, par):
                n = 2 * it + par
                sp.wait_ge(c2done, CREDIT + 2 * (n - 1))
                sp.dma_start(craw[:, par, 0, :, :], c_ri[:, :, bass.ds(n * CH, CH), :].rearrange(
                    "r n h c -> (r n) h c")).then_inc(cld[par], 16)
                for r in range(2):
                    sp.dma_start(craw[r * N:(r + 1) * N, par, 1, :, :],
                                 c_ri[1 - r, :, bass.ds(n * CH, CH), :]).then_inc(cld[par], 16)

            def store_h0(it, par):
                n = 2 * it + par
                sp.wait_ge(tokout, CREDIT + n + 1)
                sp.dma_start(h0s[bass.ds(n * CH, CH)].rearrange("(g f) c b a -> (f c b) g a", f=4),
                             tokev[:, par, :, :]).then_inc(h0st[par], 16)

            def load_h0(half):
                for par in range(2):
                    sp.wait_ge(h0st[par], CREDIT + 16 * (PAIRS // 2) * (half + 1))
                for cq in range(CQ):
                    sp.dma_start(h0[:, half, cq * TT:(cq + 1) * TT, :],
                                 h0s[half * P:(half + 1) * P, cq * TT:(cq + 1) * TT].rearrange(
                                     "h c b a -> h c (b a)")).then_inc(h0ld, 16)

            def store_q(half, cq):
                u = half * CQ + cq
                for k in range(KD):
                    sp.wait_ge(qdone, CREDIT + KD * u + k + 1)
                    sp.dma_start(qs[k, :, half, bass.ds(cq * GT, GT)], qe[:, k, :]).then_inc(qst[k], 16)

            with sp.Fori(0, PAIRS // 2) as it:
                for par in range(2):
                    load_c(it, par)
                for par in range(2):
                    store_h0(it, par)
            load_h0(0)
            with sp.Fori(PAIRS // 2, PAIRS) as it:
                for par in range(2):
                    load_c(it, par)
                for par in range(2):
                    store_h0(it, par)
                store_q(0, it - PAIRS // 2)
            load_h0(1)
            sp.wait_ge(dve_set, DVE_ALL)
            sp.wait_ge(pe_set, 2)
            for dst, src in ((fc1raw, fc1T), (fc2raw, fc2T), (projraw, projT), (wqraw, wq),
                             (leafraw, leafT), (woutraw, woutT)):
                sp.dma_start(dst[:, :, :], src.rearrange("(k p) o -> p k o", p=P)).then_inc(ld_w2, 16)
            sp.dma_start(routraw[:, :, 0:LEAVES - 1], routersT.rearrange("(k p) o -> p k o", p=P)).then_inc(
                ld_w2, 16)
            with sp.Fori(0, CQ) as cq:
                store_q(1, cq)

            sp.wait_ge(dve_set, DVE_W2)
            sp.wait_ge(act_set, 11)
            for dst, src in ((pbias, proj_b), (fc2bias, fc2_b), (woutbias, wout_b)):
                sp.dma_start(dst[:, :], src.unsqueeze(0).to_broadcast([P, D])).then_inc(ld_const, 16)
            for k in range(KD):
                sp.wait_ge(qst[k], CREDIT + 16 * GROUPS)

            def load_q(g):
                sp.wait_ge(attmm, CREDIT + g)
                for k in range(KD):
                    sp.dma_start(qf[:, k, :, :].rearrange("p (h x) t -> p h (x t)", h=HALVES),
                                 qs[k, :, :, bass.ds(g * 2 * P, 2 * P)]).then_inc(qfd, 16)

            def store_out(g):
                sp.wait_ge(outdone, CREDIT + 2 * (g + 1))
                for half in range(HALVES):
                    sp.dma_start(out[bass.ds(2 * g, 2), half * P:(half + 1) * P, :].rearrange("c p d -> p c d"),
                                 outb[:, 2 * half:2 * half + 2, :]).then_inc(outst, 16)

            load_q(0)
            load_q(1)
            with sp.Fori(2, GROUPS) as g:
                load_q(g)
                store_out(g - 2)
            store_out(GROUPS - 2)
            store_out(GROUPS - 1)
            sp.wait_ge(outst, CREDIT + 32 * GROUPS)

        @block.gpsimd
        def _(pool):
            count = [0]

            def link(ins):
                count[0] += 1
                ins.then_inc(pool_set, 1)
                pool.wait_ge(pool_set, count[0])

            link(pool.memset(Er[:, :, 0], 1.0))
            link(pool.memset(Ei[:, :, 0], 0.0))
            pool.wait_ge(dve_set, DVE_U)
            link(pool.tensor_copy(Er[:, :, 1], pw[:, 0, 0, :]))
            link(pool.tensor_copy(Ei[:, :, 1], pw[:, 0, 1, :]))
            for j, m in ((1, 2), (2, 4)):
                pool.wait_ge(dve_set, DVE_U + 4 * j)
                wr, wi = (pw[:, j, x, :].unsqueeze(2).to_broadcast([P, H, m]) for x in range(2))
                er, ei, t = Er[:, :, 0:m], Ei[:, :, 0:m], tE[:, :, 0:m]
                er2, ei2 = Er[:, :, m:2 * m], Ei[:, :, m:2 * m]
                link(pool.tensor_tensor(er2, er, wr, ALU.mult))
                link(pool.tensor_tensor(t, ei, wi, ALU.mult))
                link(pool.tensor_tensor(er2, er2, t, ALU.subtract))
                link(pool.tensor_tensor(ei2, er, wi, ALU.mult))
                link(pool.tensor_tensor(t, ei, wr, ALU.mult))
                link(pool.tensor_tensor(ei2, ei2, t, ALU.add))
            assert count[0] == POOL_TABLES, count[0]

            def rotate(it, par):
                n = 2 * it + par
                pool.wait_ge(c2done, CREDIT + 2 * (n + 1))
                ur, ui = (u128[:, x, bass.ds(n * CH, CH)].unsqueeze(2).to_broadcast([P, CH, B]) for x in range(2))
                one, two = (W[:, par, r, :, :, 0] for r in range(2))
                d1, d2 = (W[:, par, r, :, :, 1] for r in range(2))
                k = CREDIT + 6 * n
                pool.wait_ge(wdone, k)
                pool.wait_ge(tokmm, CREDIT + 2 * (n - 1))
                apart(pool)
                pool.tensor_tensor(d1, one, ur, ALU.mult).then_inc(wdone, 1)
                pool.tensor_tensor(wt[:, 0, :, :], two, ui, ALU.mult).then_inc(wdone, 1)
                pool.tensor_tensor(d2, two, ur, ALU.mult).then_inc(wdone, 1)
                pool.tensor_tensor(wt[:, 1, :, :], one, ui, ALU.mult).then_inc(wdone, 1)
                pool.wait_ge(wdone, k + 2)
                pool.tensor_tensor(d1, d1, wt[:, 0, :, :], ALU.add).then_inc(wdone, 1)
                pool.wait_ge(wdone, k + 4)
                pool.tensor_tensor(d2, d2, wt[:, 1, :, :], ALU.subtract).then_inc(wdone, 1)

            def scales(half, cq):
                u = half * CQ + cq
                pool.wait_ge(st1, CREDIT + 8 * (u + 1))
                pool.wait_ge(xh1, CREDIT + 6 * u)
                k = CREDIT + 7 * u
                v = mv1[:, :, 1]
                apart(pool)
                pool.tensor_scalar(pst1[:, 0, :], v, EPS, None, ALU.add).then_inc(r1done, 1)
                pool.wait_ge(r1done, k + 1)
                pool.tensor_tensor(pst1[:, 1, :], pst1[:, 0, :], halfpow[:, :], ALU.pow).then_inc(r1done, 1)
                pool.wait_ge(r1done, k + 2)
                pool.tensor_tensor(pst1[:, 2, :], v, pst1[:, 1, :], ALU.mult).then_inc(r1done, 1)
                pool.wait_ge(r1done, k + 3)
                pool.tensor_tensor(pst1[:, 3, :], pst1[:, 2, :], pst1[:, 1, :], ALU.mult).then_inc(r1done, 1)
                pool.wait_ge(r1done, k + 4)
                apart(pool)
                pool.tensor_scalar(pst1[:, 4, :], pst1[:, 3, :], EPS, None, ALU.add).then_inc(r1done, 1)
                pool.wait_ge(r1done, k + 5)
                pool.tensor_tensor(pst1[:, 5, :], pst1[:, 4, :], halfpow[:, :], ALU.pow).then_inc(r1done, 1)
                pool.wait_ge(r1done, k + 6)
                pool.tensor_tensor(pst1[:, 6, :], pst1[:, 5, :], pst1[:, 1, :], ALU.mult).then_inc(r1done, 1)

            pool.wait_ge(dve_set, DVE_POWERS)
            with pool.Fori(0, PAIRS // 2) as it:
                for par in range(2):
                    rotate(it, par)
            with pool.Fori(PAIRS // 2, PAIRS) as it:
                for par in range(2):
                    rotate(it, par)
                scales(0, it - PAIRS // 2)
            with pool.Fori(0, CQ) as cq:
                scales(1, cq)

            pool.wait_ge(ld_const, 16 * 9)

            def rows(bias):
                return bias[:, :].unsqueeze(1).to_broadcast([P, TT, D])

            def add_proj_bias(g):
                pool.wait_ge(x1done, CREDIT + 4 * (g + 1))
                pool.tensor_tensor(x1[:, :, :], x1[:, :, :], rows(pbias), ALU.add).then_inc(x1b, 1)

            def rstd(g, stats, per, mv, pst, used, uses, done):
                pool.wait_ge(stats, CREDIT + per * (g + 1))
                pool.wait_ge(used, CREDIT + uses * g)
                apart(pool)
                pool.tensor_scalar(pst[:, 0, :], mv[:, :, 1], EPS, None, ALU.add).then_inc(done, 1)
                pool.wait_ge(done, CREDIT + 2 * g + 1)
                pool.tensor_tensor(pst[:, 1, :], pst[:, 0, :], halfpow[:, :], ALU.pow).then_inc(done, 1)

            def residual(g):
                pool.wait_ge(h1done, CREDIT + 10 * (g - 1))
                r = r2[:, bass.ds(g % 2, 1), :, :].rearrange("p o t d -> p (o t) d")
                h = h0[:, :, bass.ds(2 * g, 2), :].rearrange("p h c d -> p h (c d)")
                x = x2[:, :, :].rearrange("p (h c) d -> p h (c d)", h=HALVES)
                r_ = r.rearrange("p (h c) d -> p h (c d)", h=HALVES)
                apart(pool)
                pool.tensor_tensor(r_, h, x, ALU.add).then_inc(r2done, 1)
                pool.wait_ge(r2done, CREDIT + 2 * g + 1)
                apart(pool)
                pool.tensor_tensor(r, r, rows(fc2bias), ALU.add).then_inc(r2done, 1)

            def out_bias(g):
                pool.wait_ge(h1done, CREDIT + 10 * (g + 1))
                pool.wait_ge(outdone, CREDIT + 2 * g)
                pool.tensor_tensor(o1[:, :, :], h1[:, :, :], rows(woutbias), ALU.add).then_inc(o1done, 1)

            def turn(it, a, m):
                if a:
                    add_proj_bias(it)
                    rstd(it, x2done, 10, mv2, pst2, xh2done, 4, v2done)
                    residual(it)
                if m:
                    rstd(it - 1, h1done, 10, mv4, pst4, x4done, 4, v4done)
                    out_bias(it - 1)

            turn(0, True, False)
            turn(1, True, True)
            with pool.Fori(2, GROUPS) as it:
                turn(it, True, True)
            turn(GROUPS, False, True)

        @block.scalar
        def _(act):
            act.wait_ge(ld_tab, 16 * 9)
            act.activation(base[:, 0, :], ldt[:, :], ACT.Exp).then_inc(act_tab, 1)
            act.activation(base[:, 1, :], iar[:, :], ACT.Exp).then_inc(act_tab, 1)

            def operands(it, par):
                n = 2 * it + par
                act.wait_ge(cld[par], CREDIT + 48 * (it + 1))
                act.wait_ge(tokmm, CREDIT + 2 * (n - 1))
                act.activation(W[:, par, 0, :, :, 0], craw[:, par, 0, :, :], ACT.Copy).then_inc(c2done, 1)
                act.activation(W[:, par, 1, :, :, 0], craw[:, par, 1, :, :], ACT.Copy, scale=sgn[:, 0:1]).then_inc(
                    c2done, 1)

            def token_out(it, par):
                n = 2 * it + par
                act.wait_ge(tokmm, CREDIT + 2 * (n + 1))
                act.wait_ge(h0st[par], CREDIT + 16 * it)
                act.activation(tokev[:, par, :, :], bank(par), ACT.Copy).then_inc(tokout, 1)

            def y_high(half, cq):
                u = half * CQ + cq
                act.wait_ge(yT, CREDIT + u + 1)
                act.wait_ge(kvmm, CREDIT + TT * u)
                for k in range(KD):
                    act.activation(yh[:, k, :], bank(2 + k), ACT.Copy).then_inc(yhd, 1)

            def q_parts(half, cq):
                u = half * CQ + cq
                for o in range(KD):
                    act.wait_ge(qmm, CREDIT + KD * u + o + 1)
                    act.wait_ge(qst[o], CREDIT + 16 * u)
                    act.activation(qe[:, o, :], bank(4 + o), ACT.Exp, bias=qbias[:, o:o + 1]).then_inc(qact, 1)
                    act.activation(qr[:, o, :], bank(4 + o), ACT.Relu, bias=qbias[:, o:o + 1]).then_inc(qact, 1)

            def kv_parts(half, cq):
                u = half * CQ + cq
                for t in range(TT):
                    b = (6, 4, 5, 6)[t]
                    act.wait_ge(kvmm, CREDIT + TT * u + t + 1)
                    act.wait_ge(kdone, CREDIT + TT * u + t - 1)
                    act.wait_ge(ksmm, CREDIT + TT * u + t - 1)
                    act.activation(ke[:, t % 2, :], PS[:, b, 0:D], ACT.Exp).then_inc(kvact, 1)
                    act.activation(kr[:, t % 2, :], PS[:, b, 0:D], ACT.Relu).then_inc(kvact, 1)
                    act.activation(vt[:, t % 2, :, 0:P], PS[:, b, D:2 * D].rearrange("p (k c) -> p k c", k=KD),
                                   ACT.Copy).then_inc(kvact, 1)

            act.wait_ge(dve_set, DVE_TABLES)
            with act.Fori(0, PAIRS // 2) as it:
                for par in range(2):
                    operands(it, par)
                for par in range(2):
                    token_out(it, par)
            act.wait_ge(dve_set, DVE_QKV)
            act.activation(qkvh[:, :, :], qkvraw[:, :, :], ACT.Copy).then_inc(act_set, 1)
            act.activation(kvbh[:, :], PS[0:N, 6, :], ACT.Copy).then_inc(act_set, 1)
            act.activation(kvb[0:32, :], PS[0:32, 6, :], ACT.Copy).then_inc(act_set, 1)
            act.activation(qbias[:, :], PS[:, 7, 0:KD], ACT.Copy).then_inc(act_set, 1)
            act.wait_ge(act_set, 4)
            with act.Fori(PAIRS // 2, PAIRS) as it:
                for par in range(2):
                    operands(it, par)
                token_out(it, 0)
                y_high(0, it - PAIRS // 2)
                token_out(it, 1)
                q_parts(0, it - PAIRS // 2)
                kv_parts(0, it - PAIRS // 2)
            with act.Fori(0, CQ) as cq:
                y_high(1, cq)
                q_parts(1, cq)
                kv_parts(1, cq)

            act.wait_ge(dve_set, DVE_FC1)
            act.wait_ge(tokmm, CREDIT + 2 * CHUNKS)
            act.wait_ge(vdone, CREDIT + 4 * CHUNKS)
            act.activation(fc1h[:, :, :], fc1raw[:, :, :], ACT.Copy).then_inc(act_set, 1)
            act.activation(fc2h[:, :, :], fc2raw[:, :, :], ACT.Copy).then_inc(act_set, 1)
            act.activation(projh[:, :, :], projraw[:, :, :], ACT.Copy).then_inc(act_set, 1)
            act.wait_ge(pe_set, 5)
            for k in range(KD):
                act.activation(gateh[:, k, :], PS[:, 4 + k, 0:LEAVES], ACT.Copy).then_inc(act_set, 1)
            for k in range(KD):
                act.activation(leafh[:, k, :], PS[:, 6 + k, 0:D], ACT.Copy, scale=2.0 ** -LEVELS).then_inc(
                    act_set, 1)

            def high(dst, b, made, g, used, uses, done):
                act.wait_ge(made, CREDIT + g + 1)
                act.wait_ge(used, CREDIT + uses)
                for k in range(KD):
                    act.activation(dst(k), bank(b + k), ACT.Copy).then_inc(done, 1)

            def gelu(g, j):
                n = JH * g + j
                act.wait_ge(f1mm, CREDIT + n + 1)
                act.wait_ge(gldone, CREDIT + n - 1)
                act.activation(gf[:, j % 2, :], bank(j % 2), ACT.Gelu, bias=fc1bias[:, j:j + 1]).then_inc(gact, 1)
                act.wait_ge(gact, CREDIT + 2 * n + 1)
                act.wait_ge(f2mm, CREDIT + n - 1)
                act.activation(gh[:, j % 2, :], gf[:, j % 2, :], ACT.Copy).then_inc(gact, 1)

            def turn(it, a, m, f):
                par = it % 2

                def mlp(j):
                    if m:
                        gelu(it - 1, j)

                mlp(0)
                mlp(1)
                if a:
                    high(lambda k: aTh[:, k, :], 4, attT, it, prmm, it, attTh)
                mlp(2)
                if f:
                    high(lambda k: x4Th[:, k, :], 6, x4T, it - 2, gtmm, it - 2, x4Thd)
                mlp(3)
                if f:
                    act.wait_ge(gtmm, CREDIT + it - 1)
                    act.wait_ge(tree, CREDIT + 16 * (it - 2))
                    for b in range(2):
                        act.activation(th[:, 2 * b:2 * b + 2, :], bank(6 + b), ACT.Tanh, scale=0.5).then_inc(
                            thdone, 1)
                mlp(4)
                mlp(5)
                if a:
                    high(lambda k: x2Th[:, bass.ds(par, 1), k, :].rearrange("p o t -> p (o t)"), 4, x2T, it,
                         f1mm, JH * (it - 1), x2Thd)
                mlp(6)
                if f:
                    high(lambda k: lTh[:, k, :], 6, lT, it - 2, lvmm, it - 2, lThd)
                mlp(7)

            turn(0, True, False, False)
            turn(1, True, True, False)
            with act.Fori(2, GROUPS) as it:
                turn(it, True, True, True)
            turn(GROUPS, False, True, True)
            turn(GROUPS + 1, False, False, True)

        @block.vector
        def _(dve):
            count = [0]

            def link(ins):
                count[0] += 1
                ins.then_inc(dve_set, 1)
                dve.wait_ge(dve_set, count[0])

            def tt(out_, a, b, op):
                link(dve.tensor_tensor(out_, a, b, op))

            link(dve.memset(sgn[0:N, 0:1], -1.0))
            link(dve.memset(sgn[N:P, 0:1], 1.0))
            link(dve.memset(sgn[0:N, 1:2], 2.0))
            link(dve.memset(sgn[N:P, 1:2], -2.0))
            link(dve.memset(ones[:, :], 1.0))
            link(dve.memset(halfpow[:, :], -0.5))
            dve.wait_ge(act_tab, 2)
            dt, ea = base[:, 0, :], base[:, 1, :]
            zr, zi, omz, t0, den, t1, nr = (base[:, k, :] for k in range(2, 9))
            link(dve.scalar_tensor_tensor(zr, ea, -0.5, dt, ALU.mult, ALU.mult))
            link(dve.scalar_tensor_tensor(zi, aim[:, :], 0.5, dt, ALU.mult, ALU.mult))
            link(dve.tensor_scalar(omz, zr, -1.0, 1.0, ALU.mult, ALU.add))
            tt(t0, zi, zi, ALU.mult)
            tt(den, omz, omz, ALU.mult)
            tt(den, den, t0, ALU.add)
            link(dve.reciprocal(t1, den))
            link(dve.scalar_tensor_tensor(nr, zr, 1.0, omz, ALU.add, ALU.mult))
            tt(nr, nr, t0, ALU.subtract)
            tt(pw[:, 0, 0, :], nr, t1, ALU.mult)
            link(dve.scalar_tensor_tensor(pw[:, 0, 1, :], zi, 2.0, t1, ALU.mult, ALU.mult))
            assert count[0] == DVE_U, count[0]
            for j in range(LOGS - 1):
                wr, wi = pw[:, j, 0, :], pw[:, j, 1, :]
                dr, di = (u128[:, x, :] if j == LOGS - 2 else pw[:, j + 1, x, :] for x in range(2))
                tt(t0, wr, wr, ALU.mult)
                tt(t1, wi, wi, ALU.mult)
                tt(dr, t0, t1, ALU.subtract)
                link(dve.scalar_tensor_tensor(di, wr, 2.0, wi, ALU.mult, ALU.mult))
            assert count[0] == DVE_POWERS, count[0]

            link(dve.tensor_scalar(X[:, :, 0], btab[:, 0, :], sgn[:, 1:2], None, ALU.mult))
            link(dve.tensor_scalar(Y[:, :, 0], btab[:, 1, :], -2.0, None, ALU.mult))
            for j, m in ((3, 1), (4, 2), (5, 4), (6, 8)):
                wr, wi = (pw[:, j, x, :].unsqueeze(2).to_broadcast([P, H, m]) for x in range(2))
                x, y, t, x_ = X[:, :, 0:m], Y[:, :, 0:m], tX[:, :, 0:m], X[:, :, m:2 * m]
                tt(x_, x, wr, ALU.mult)
                tt(t, y, wi, ALU.mult)
                tt(x_, x_, t, ALU.add)
                if m < NE:
                    y_ = Y[:, :, m:2 * m]
                    tt(y_, y, wr, ALU.mult)
                    tt(t, x, wi, ALU.mult)
                    tt(y_, y_, t, ALU.subtract)
            assert count[0] == DVE_TABLES, count[0]

            def products(it, par):
                for s in range(2):
                    q = 2 * (2 * it + par) + s
                    dve.wait_ge(tokmm, CREDIT + q - 1)
                    x = X[:, bass.ds(q * SUB, SUB), :].unsqueeze(3).to_broadcast([P, SUB, NA, NE])
                    for r, e in enumerate((Er, Ei)):
                        w = e[:, bass.ds(q * SUB, SUB), :].unsqueeze(2).to_broadcast([P, SUB, NA, NE])
                        dve.tensor_tensor(prods[:, s, r, :, :].rearrange("p h (a e) -> p h a e", a=NA), x, w,
                                          ALU.mult).then_inc(vdone, 1)

            def norm1(half, cq):
                u = half * CQ + cq

                def tile(t):
                    return h0[:, half, bass.ds(cq * TT + t, 1), :].rearrange("p o d -> p (o d)")

                dve.wait_ge(xh1, CREDIT + 6 * u)
                for t in range(TT):
                    dve.bn_stats(bst1[:, t, :], tile(t)).then_inc(st1, 1)
                dve.wait_ge(st1, CREDIT + 8 * u + TT)
                apart(dve)
                for t in range(TT):
                    dve.bn_aggr(mv1[:, t, :], bst1[:, t, :]).then_inc(st1, 1)
                dve.wait_ge(st1, CREDIT + 8 * (u + 1))
                dve.wait_ge(r1done, CREDIT + 7 * (u + 1))
                dve.wait_ge(yT, CREDIT + u)
                for t in range(TT):
                    dve.tensor_scalar(xh[:, t, :], tile(t), mv1[:, t, 0:1], pst1[:, 6, t:t + 1],
                                      ALU.subtract, ALU.mult).then_inc(xh1, 1)
                dve.tensor_copy(mr[:, 0, half, bass.ds(cq * TT, TT)], mv1[:, :, 0]).then_inc(xh1, 1)
                dve.tensor_copy(mr[:, 1, half, bass.ds(cq * TT, TT)], pst1[:, 1, :]).then_inc(xh1, 1)

            def y_low(half, cq):
                u = half * CQ + cq
                dve.wait_ge(kvmm, CREDIT + TT * u)
                for k in range(KD):
                    dve.wait_ge(yhd, CREDIT + KD * u + k + 1)
                    dve.tensor_tensor(yl[:, k, :], bank(2 + k), yh[:, k, :].bitcast(F32),
                                      ALU.subtract).then_inc(yld, 1)

            def q_elu(half, cq):
                u = half * CQ + cq
                for o in range(KD):
                    dve.wait_ge(qact, CREDIT + 2 * (KD * u + o + 1))
                    dve.scalar_tensor_tensor(qe[:, o, :], qe[:, o, :], 1.0, qr[:, o, :], ALU.min,
                                             ALU.add).then_inc(qdone, 1)

            def k_elu(half, cq, t):
                n = TT * (half * CQ + cq) + t
                dve.wait_ge(kvact, CREDIT + 3 * n + 2)
                dve.wait_ge(ksmm, CREDIT + n - 1)
                dve.scalar_tensor_tensor(kt[:, t % 2, :], ke[:, t % 2, :], 1.0, kr[:, t % 2, :], ALU.min,
                                         ALU.add).then_inc(kdone, 1)

            def kv_sum(half, cq, t):
                n = TT * (half * CQ + cq) + t
                c = TT * cq + t
                raw = kvraw[:, bass.ds(c, 1), :, :].rearrange("p o k x -> p (o k) x")
                new = PS[:, 7, 0:KD * (P + 1)].rearrange("p (k x) -> p k x", k=KD)
                dve.wait_ge(ksmm, CREDIT + n + 1)
                if half == 0:
                    dve.tensor_copy(raw, new).then_inc(ksum0, 1)
                    return
                k = CREDIT + 3 * c
                dve.wait_ge(ksum1, k)
                dve.tensor_tensor(kvs[:, :, :], new, raw, ALU.add).then_inc(ksum1, 1)
                dve.wait_ge(ksum1, k + 1)
                m = kvm[:, bass.ds(c, 1), :, :].rearrange("p o k x -> p (o k) x")
                dve.tensor_tensor(m[:, :, 0:P], kvs[:, :, 0:P], mask.unsqueeze(1).to_broadcast([P, KD, P]),
                                  ALU.mult).then_inc(ksum1, 1)
                dve.tensor_tensor(m[:, :, P:QW], kvs[:, :, P:P + 1].to_broadcast([P, KD, HPB]),
                                  mask8.unsqueeze(1).to_broadcast([P, KD, HPB]), ALU.mult).then_inc(ksum1, 1)

            def keys(half, cq):
                for t in range(TT):
                    k_elu(half, cq, t)
                    if t:
                        kv_sum(half, cq, t - 1)
                kv_sum(half, cq, TT - 1)

            dve.wait_ge(pool_set, POOL_TABLES)
            with dve.Fori(0, PAIRS // 2) as it:
                for par in range(2):
                    products(it, par)

            dve.wait_ge(ld_const, 16 * 6)
            dve.wait_ge(ld_qkv, 16)
            link(dve.memset(bcol[:, :, :], 0.0))
            link(dve.tensor_copy(bcol[:, :, 0], nrm[:, 1, :]))
            link(dve.tensor_copy(bcol[:, :, 32], nrm[:, 1, :]))
            link(dve.tensor_copy(onesr[:, :], ones[0:N, :]))
            link(dve.tensor_copy(vt[:, :, :, P], ones[:, 0:2 * KD].rearrange("p (a k) -> p a k", a=2)))
            assert count[0] == DVE_BCOL
            dve.wait_ge(pe_set, 2)
            for k in range(KD):
                link(dve.tensor_scalar(qkvraw[:, k, :], qkvraw[:, k, :], nrm[:, 0, k:k + 1], None, ALU.mult))
            assert count[0] == DVE_QKV
            dve.wait_ge(act_set, 4)
            tt(qkvl[:, :, :], qkvraw[:, :, :], qkvh[:, :, :].bitcast(F32), ALU.subtract)
            tt(kvb[32:N, :], PS[32:N, 6, :], kvbh[32:N, :].bitcast(F32), ALU.subtract)
            assert count[0] == DVE_ALL

            dve.wait_ge(h0ld, 16 * CQ)
            with dve.Fori(PAIRS // 2, PAIRS) as it:
                cq = it - PAIRS // 2
                products(it, 0)
                norm1(0, cq)
                products(it, 1)
                y_low(0, cq)
                q_elu(0, cq)
                keys(0, cq)
            dve.wait_ge(ksum0, CREDIT + B)
            dve.wait_ge(h0ld, 2 * 16 * CQ)
            with dve.Fori(0, CQ) as cq:
                norm1(1, cq)
                y_low(1, cq)
                q_elu(1, cq)
                keys(1, cq)

            dve.wait_ge(ld_w2, 16 * 7)
            link(dve.memset(routraw[:, :, LEAVES - 1:LEAVES], 0.0))
            assert count[0] == DVE_ROUT
            dve.wait_ge(pe_set, 3)
            tt(fc1bias[:, :], fc1bias[:, :], PS[:, 0, 0:JH], ALU.add)
            for k in range(KD):
                link(dve.tensor_scalar(fc1raw[:, k, :], fc1raw[:, k, :], nrm[:, 2, k:k + 1], None, ALU.mult))
            assert count[0] == DVE_FC1
            dve.wait_ge(act_set, 7)
            tt(fc1l[:, :, :], fc1raw[:, :, :], fc1h[:, :, :].bitcast(F32), ALU.subtract)
            tt(fc2l[:, :, :], fc2raw[:, :, :], fc2h[:, :, :].bitcast(F32), ALU.subtract)
            tt(projl[:, :, :], projraw[:, :, :], projh[:, :, :].bitcast(F32), ALU.subtract)
            dve.wait_ge(act_set, 11)
            for k in range(KD):
                tt(gatel[:, k, :], PS[:, 4 + k, 0:LEAVES], gateh[:, k, :].bitcast(F32), ALU.subtract)
            for k in range(KD):
                link(dve.scalar_tensor_tensor(leafl[:, k, :], PS[:, 6 + k, 0:D], 2.0 ** -LEVELS,
                                              leafh[:, k, :].bitcast(F32), ALU.mult, ALU.subtract))
            assert count[0] == DVE_W2, count[0]

            def one_tile(g, t):
                return h0[:, t // 2, bass.ds(2 * g + t % 2, 1), :].rearrange("p o d -> p (o d)")

            def attention(g):
                dve.wait_ge(attmm, CREDIT + g + 1)
                k = CREDIT + 7 * g
                dve.wait_ge(attdone, k)
                for b in range(3):
                    n = min(3, TT * KD - 3 * b)
                    r = PS[:, 4 + b, 0:n * QW].rearrange("p (r x) -> p r x", x=QW)
                    dve.tensor_scalar(zden[:, 3 * b:3 * b + n, :], r[:, :, P:QW], EPS_ATTN, None,
                                      ALU.add).then_inc(attdone, 1)
                dve.wait_ge(attdone, k + 3)
                dve.reciprocal(zrec[:, :, :], zden[:, :, :]).then_inc(attdone, 1)
                dve.wait_ge(attdone, k + 4)
                dve.wait_ge(x2T, CREDIT + g)
                regions = att[:, :, :].rearrange("p t (k c) -> p (t k) c", k=KD)
                for b in range(3):
                    n = min(3, TT * KD - 3 * b)
                    r = PS[:, 4 + b, 0:n * QW].rearrange("p (r x) -> p r x", x=QW)
                    dve.tensor_tensor(regions[:, 3 * b:3 * b + n, :].rearrange("p r (h e) -> p r h e", h=HPB),
                                      r[:, :, 0:P].rearrange("p r (h e) -> p r h e", h=HPB),
                                      zrec[:, 3 * b:3 * b + n, :].unsqueeze(3).to_broadcast([P, n, HPB, HD]),
                                      ALU.mult).then_inc(attdone, 1)

            def remake_x1(g):
                dve.wait_ge(x2done, CREDIT + 10 * g)
                for t in range(TT):
                    m, r = (mr[:, x, t // 2, bass.ds(2 * g + t % 2, 1)] for x in range(2))
                    dve.tensor_scalar(x1[:, t, :], one_tile(g, t), m, r, ALU.subtract, ALU.mult).then_inc(
                        x1done, 1)

            def low(dst, high, b, used, uses, hdone, g, done):
                dve.wait_ge(used, CREDIT + uses)
                for k in range(KD):
                    dve.wait_ge(hdone, CREDIT + KD * g + k + 1)
                    dve.tensor_tensor(dst(k), bank(b + k), high(k).bitcast(F32), ALU.subtract).then_inc(done, 1)

            def stats(x, bst, mv, done, k):
                dve.wait_ge(done, k)
                for t in range(TT):
                    dve.bn_stats(bst[:, t, :], x[:, t, :]).then_inc(done, 1)
                dve.wait_ge(done, k + TT)
                apart(dve)
                for t in range(TT):
                    dve.bn_aggr(mv[:, t, :], bst[:, t, :]).then_inc(done, 1)

            def residual2(g):
                dve.wait_ge(prmm, CREDIT + g + 1)
                dve.wait_ge(x1b, CREDIT + g + 1)
                dve.wait_ge(r2done, CREDIT + 2 * g - 1)
                dve.wait_ge(xh2done, CREDIT + 4 * g)
                for b in range(2):
                    dve.tensor_tensor(x2[:, 2 * b:2 * b + 2, :], PS[:, 4 + b, :].rearrange("p (t d) -> p t d", t=2),
                                      x1[:, 2 * b:2 * b + 2, :], ALU.add).then_inc(x2done, 1)
                stats(x2, bst2, mv2, x2done, CREDIT + 10 * g + 2)

            def normalize(dst, x, mv, pst, g, stats_, scale, used, uses, done):
                dve.wait_ge(stats_, CREDIT + 10 * (g + 1))
                dve.wait_ge(scale, CREDIT + 2 * (g + 1))
                dve.wait_ge(used, CREDIT + uses)
                for t in range(TT):
                    dve.tensor_scalar(dst[:, t, :], x[:, t, :], mv[:, t, 0:1], pst[:, 1, t:t + 1],
                                      ALU.subtract, ALU.mult).then_inc(done, 1)

            def gelu_low(g, j):
                n = JH * g + j
                dve.wait_ge(gact, CREDIT + 2 * (n + 1))
                dve.wait_ge(f2mm, CREDIT + n - 1)
                dve.tensor_tensor(gl[:, j % 2, :], gf[:, j % 2, :], gh[:, j % 2, :].bitcast(F32),
                                  ALU.subtract).then_inc(gldone, 1)

            def leaf_probabilities(g):
                k = CREDIT + 16 * g
                dve.wait_ge(tree, k)
                dve.wait_ge(thdone, CREDIT + 2 * (g + 1))
                dve.wait_ge(lT, CREDIT + g)
                dve.tensor_scalar(lpA[:, :, 1:2], th[:, :, 0:1], 1.0, None, ALU.add).then_inc(tree, 1)
                dve.tensor_scalar(lpA[:, :, 0:1], th[:, :, 0:1], -1.0, 1.0, ALU.mult, ALU.add).then_inc(tree, 1)
                for level in range(1, LEVELS):
                    n = 2 ** level
                    src, dst = ((lpA, lpB), (lpB, lpA))[level % 2 == 0]
                    pairs = dst[:, :, 0:2 * n].rearrange("p t (n s) -> p t n s", s=2)
                    nodes = src[:, :, 0:n]
                    dve.wait_ge(tree, k + 2 * level)
                    dve.scalar_tensor_tensor(pairs[:, :, :, 1], th[:, :, n - 1:2 * n - 1], 1.0, nodes,
                                             ALU.add, ALU.mult).then_inc(tree, 1)
                    dve.wait_ge(tree, k + 2 * level + 1)
                    dve.scalar_tensor_tensor(pairs[:, :, :, 0], nodes, 2.0, pairs[:, :, :, 1],
                                             ALU.mult, ALU.subtract).then_inc(tree, 1)

            def finish(g):
                dve.wait_ge(lvmm, CREDIT + g + 1)
                dve.wait_ge(o1done, CREDIT + g + 1)
                dve.wait_ge(outst, CREDIT + 32 * g)
                for b in range(2):
                    dve.tensor_tensor(outb[:, 2 * b:2 * b + 2, :],
                                      PS[:, 6 + b, :].rearrange("p (t d) -> p t d", t=2),
                                      o1[:, 2 * b:2 * b + 2, :], ALU.add).then_inc(outdone, 1)

            def after_mlp(g):
                dve.wait_ge(f2mm, CREDIT + JH * (g + 1))
                dve.wait_ge(r2done, CREDIT + 2 * (g + 1))
                dve.wait_ge(o1done, CREDIT + g)
                dve.wait_ge(x4done, CREDIT + 4 * g)
                r = r2[:, bass.ds(g % 2, 1), :, :].rearrange("p o t d -> p (o t) d")
                for b in range(2):
                    dve.tensor_tensor(h1[:, 2 * b:2 * b + 2, :], PS[:, 2 + b, :].rearrange("p (t d) -> p t d", t=2),
                                      r[:, 2 * b:2 * b + 2, :], ALU.add).then_inc(h1done, 1)
                stats(h1, bst4, mv4, h1done, CREDIT + 10 * g + 2)

            def turn(it, a, m, f):
                buf = bass.ds(it % 2, 1)

                def mlp(j):
                    if m:
                        gelu_low(it - 1, j)

                mlp(0)
                if a:
                    attention(it)
                mlp(1)
                if a:
                    remake_x1(it)
                    low(lambda k: aTl[:, k, :], lambda k: aTh[:, k, :], 4, prmm, it, attTh, it, attTl)
                mlp(2)
                if f:
                    low(lambda k: x4Tl[:, k, :], lambda k: x4Th[:, k, :], 6, gtmm, it - 2, x4Thd, it - 2, x4Tld)
                mlp(3)
                if a:
                    residual2(it)
                mlp(4)
                if f:
                    leaf_probabilities(it - 2)
                if a:
                    normalize(xh2, x2, mv2, pst2, it, x2done, v2done, attT, it + 1, xh2done)
                mlp(5)
                if a:
                    low(lambda k: x2Tl[:, buf, k, :].rearrange("p o t -> p (o t)"),
                        lambda k: x2Th[:, buf, k, :].rearrange("p o t -> p (o t)"),
                        4, f1mm, JH * (it - 1), x2Thd, it, x2Tld)
                mlp(6)
                if f:
                    low(lambda k: lTl[:, k, :], lambda k: lTh[:, k, :], 6, lvmm, it - 2, lThd, it - 2, lTld)
                mlp(7)
                if f:
                    finish(it - 2)
                if m:
                    after_mlp(it - 1)
                    normalize(x4, h1, mv4, pst4, it - 1, h1done, v4done, x4T, it - 1, x4done)

            turn(0, True, False, False)
            turn(1, True, True, False)
            with dve.Fori(2, GROUPS) as it:
                turn(it, True, True, True)
            turn(GROUPS, False, True, True)
            turn(GROUPS + 1, False, False, True)

        @block.tensor
        def _(pe):
            def tokens(it, par):
                n = 2 * it + par
                pe.wait_ge(wdone, CREDIT + 6 * (n + 1))
                pe.wait_ge(c2done, CREDIT + 2 * (n + 1))
                pe.wait_ge(tokout, CREDIT + n - 1)
                for s in range(2):
                    pe.wait_ge(vdone, CREDIT + 2 * (2 * n + s + 1))
                    for i in range(SUB):
                        h = s * SUB + i
                        rows = slice(32 * (h % 4), 32 * (h % 4) + 32)
                        dst = PS[rows, par, (h // 4) * P:(h // 4 + 1) * P]
                        for r in range(2):
                            w = W[:, par, r, h, :, :].rearrange("p c b -> p (c b)")
                            mm = pe.matmul(dst, w, prods[:, s, r, i, :], start=r == 0, stop=r == 1)
                    mm.then_inc(tokmm, 1)

            def transposes(src, b, done):
                for k in range(KD):
                    for t in range(TT):
                        mm = pe.transpose(PS[:, b + k, t * P:(t + 1) * P], src[:, t, k * P:(k + 1) * P], ident)
                mm.then_inc(done, 1)

            def y_transposes(half, cq):
                u = half * CQ + cq
                pe.wait_ge(xh1, CREDIT + 6 * u + 4)
                pe.wait_ge(yld, CREDIT + KD * u)
                transposes(xh, 2, yT)

            def q_products(half, cq):
                u = half * CQ + cq
                pe.wait_ge(yld, CREDIT + KD * (u + 1))
                pe.wait_ge(yhd, CREDIT + KD * (u + 1))
                for o in range(KD):
                    pe.wait_ge(kvact, CREDIT + 3 * (TT * (u - 1) + 2 + o))
                    for k in range(KD):
                        w = slice(o * P, (o + 1) * P)
                        mm = three(pe, bank(4 + o), qkvh[:, k, w], qkvl[:, k, w], yh[:, k, :], yl[:, k, :],
                                   k == 0, k == KD - 1)
                    mm.then_inc(qmm, 1)

            def kv_products(half, cq, t):
                u = half * CQ + cq
                if t in (0, 3):
                    pe.wait_ge(kvact, CREDIT + 3 * (TT * u + (1 if t else 0)))
                else:
                    pe.wait_ge(qact, CREDIT + 2 * (KD * u + t))
                b = (6, 4, 5, 6)[t]
                pe.matmul(bank(b), onesr[:, :], kvb[:, :], start=True, stop=False)
                for k in range(KD):
                    x = slice(t * P, (t + 1) * P)
                    mm = three(pe, bank(b), yh[:, k, x], yl[:, k, x], qkvh[:, k, D:3 * D], qkvl[:, k, D:3 * D],
                               False, k == KD - 1)
                mm.then_inc(kvmm, 1)

            def kv_sums(half, cq, t):
                n = TT * (half * CQ + cq) + t
                c = TT * cq + t
                pe.wait_ge(kdone, CREDIT + n + 1)
                pe.wait_ge(kvact, CREDIT + 3 * (n + 1))
                if half == 0:
                    pe.wait_ge(ksum0, CREDIT + c)
                else:
                    pe.wait_ge(ksum1, CREDIT + 3 * c)
                for k in range(KD):
                    mm = pe.matmul(PS[:, 7, k * (P + 1):(k + 1) * (P + 1)], kt[:, t % 2, k * P:(k + 1) * P],
                                   vt[:, t % 2, k, :], start=True, stop=True)
                mm.then_inc(ksmm, 1)

            def group(half, cq):
                q_products(half, cq)
                kv_products(half, cq, 0)
                for t in range(TT):
                    if t + 1 < TT:
                        kv_products(half, cq, t + 1)
                    kv_sums(half, cq, t)

            with pe.Fori(0, PAIRS // 2) as it:
                for par in range(2):
                    tokens(it, par)

            pe.wait_ge(dve_set, DVE_BCOL)
            for k in range(KD):
                mm = pe.matmul(PS[0:N, 6, :], bcol[:, k, :], qkvraw[:, k, D:3 * D], start=k == 0,
                               stop=k == KD - 1)
            mm.then_inc(pe_set, 1)
            for o in range(KD):
                for k in range(KD):
                    mm = pe.matmul(PS[:, 7, o:o + 1], qkvraw[:, k, o * P:(o + 1) * P], nrm[:, 1, k:k + 1],
                                   start=k == 0, stop=k == KD - 1)
            mm.then_inc(pe_set, 1)
            pe.wait_ge(dve_set, DVE_ALL)
            pe.wait_ge(act_set, 4)

            with pe.Fori(PAIRS // 2, PAIRS) as it:
                tokens(it, 0)
                y_transposes(0, it - PAIRS // 2)
                tokens(it, 1)
                group(0, it - PAIRS // 2)
            pe.wait_ge(ksum0, CREDIT + B)
            with pe.Fori(0, CQ) as cq:
                y_transposes(1, cq)
                group(1, cq)

            pe.wait_ge(ld_w2, 16 * 7)
            pe.wait_ge(tokout, CREDIT + CHUNKS)
            for j in range(JH):
                for k in range(KD):
                    mm = pe.matmul(PS[:, 0, j:j + 1], fc1raw[:, k, j * P:(j + 1) * P], nrm[:, 3, k:k + 1],
                                   start=k == 0, stop=k == KD - 1)
            mm.then_inc(pe_set, 1)
            pe.wait_ge(dve_set, DVE_ROUT)
            pe.wait_ge(kvact, CREDIT + 3 * TT * GROUPS)
            pe.wait_ge(ksum1, CREDIT + 3 * B)
            for o in range(KD):
                for k in range(KD):
                    mm = pe.matmul(PS[:, 4 + o, 0:LEAVES], wqraw[:, k, o * P:(o + 1) * P], routraw[:, k, :],
                                   start=k == 0, stop=k == KD - 1)
            mm.then_inc(pe_set, 1)
            for o in range(KD):
                for k in range(KD):
                    mm = pe.matmul(PS[:, 6 + o, 0:D], leafraw[:, k, o * P:(o + 1) * P], woutraw[:, k, :],
                                   start=k == 0, stop=k == KD - 1)
            mm.then_inc(pe_set, 1)
            pe.wait_ge(dve_set, DVE_W2)
            pe.wait_ge(act_set, 11)

            def attention(g):
                pe.wait_ge(qfd, CREDIT + 32 * (g + 1))
                pe.wait_ge(x2Tld, CREDIT + KD * g)
                pe.wait_ge(outdone, CREDIT + 2 * (g - 2))
                for t in range(TT):
                    for k in range(KD):
                        r = t * KD + k
                        kv = kvm[:, bass.ds(2 * g + t % 2, 1), k, :].rearrange("p o x -> p (o x)")
                        mm = pe.matmul(PS[:, 4 + r // 3, (r % 3) * QW:(r % 3 + 1) * QW], qf[:, k, t, :], kv,
                                       start=True, stop=True)
                mm.then_inc(attmm, 1)

            def rows_out(b, ah, al, wh, wl, done):
                for t in range(TT):
                    x = slice(t * P, (t + 1) * P)
                    for k in range(KD):
                        mm = three(pe, PS[:, b + t // 2, (t % 2) * D:(t % 2 + 1) * D], ah[:, k, x], al[:, k, x],
                                   wh[:, k, :], wl[:, k, :], k == 0, k == KD - 1)
                mm.then_inc(done, 1)

            def fc1(g, j):
                n = JH * g + j
                if j == 0:
                    pe.wait_ge(x2Tld, CREDIT + KD * (g + 1))
                    pe.wait_ge(x2Thd, CREDIT + KD * (g + 1))
                pe.wait_ge(gact, CREDIT + 2 * n - 3)
                w = slice(j * P, (j + 1) * P)
                buf = bass.ds(g % 2, 1)
                for k in range(KD):
                    xh_, xl_ = (x[:, buf, k, :].rearrange("p o t -> p (o t)") for x in (x2Th, x2Tl))
                    mm = three(pe, bank(j % 2), fc1h[:, k, w], fc1l[:, k, w], xh_, xl_, k == 0, k == KD - 1)
                mm.then_inc(f1mm, 1)

            def fc2(g, j):
                n = JH * g + j
                if j == 0:
                    pe.wait_ge(h1done, CREDIT + 10 * g - 8)
                pe.wait_ge(gact, CREDIT + 2 * (n + 1))
                pe.wait_ge(gldone, CREDIT + n + 1)
                for t in range(TT):
                    x = slice(t * P, (t + 1) * P)
                    mm = three(pe, PS[:, 2 + t // 2, (t % 2) * D:(t % 2 + 1) * D], gh[:, j % 2, x],
                               gl[:, j % 2, x], fc2h[:, j, :], fc2l[:, j, :], j == 0 and t % 2 == 0,
                               j == JH - 1, skip_group_check=True)
                mm.then_inc(f2mm, 1)

            def turn(it, a, m, f):
                g = it - 1
                if m:
                    fc1(g, 0)
                if a:
                    attention(it)
                if m:
                    fc1(g, 1)
                    fc2(g, 0)
                if a:
                    pe.wait_ge(attdone, CREDIT + 7 * (it + 1))
                    transposes(att, 4, attT)
                if m:
                    fc1(g, 2)
                    fc2(g, 1)
                if f:
                    pe.wait_ge(x4done, CREDIT + 4 * (it - 1))
                    pe.wait_ge(outdone, CREDIT + 2 * (it - 2))
                    transposes(x4, 6, x4T)
                if m:
                    fc1(g, 3)
                if a:
                    pe.wait_ge(attTl, CREDIT + KD * (it + 1))
                    pe.wait_ge(attTh, CREDIT + KD * (it + 1))
                    rows_out(4, aTh, aTl, projh, projl, prmm)
                if m:
                    fc2(g, 2)
                if f:
                    pe.wait_ge(x4Tld, CREDIT + KD * (it - 1))
                    pe.wait_ge(x4Thd, CREDIT + KD * (it - 1))
                    rows_out(6, x4Th, x4Tl, gateh, gatel, gtmm)
                if m:
                    fc1(g, 4)
                    fc2(g, 3)
                    fc1(g, 5)
                    fc2(g, 4)
                if a:
                    pe.wait_ge(xh2done, CREDIT + 4 * (it + 1))
                    transposes(xh2, 4, x2T)
                if m:
                    fc1(g, 6)
                    fc2(g, 5)
                if f:
                    pe.wait_ge(tree, CREDIT + 16 * (it - 1))
                    transposes(lpB, 6, lT)
                if m:
                    fc1(g, 7)
                    fc2(g, 6)
                if f:
                    pe.wait_ge(lTld, CREDIT + KD * (it - 1))
                    pe.wait_ge(lThd, CREDIT + KD * (it - 1))
                    rows_out(6, lTh, lTl, leafh, leafl, lvmm)
                if m:
                    fc2(g, 7)

            turn(0, True, False, False)
            turn(1, True, True, False)
            with pe.Fori(2, GROUPS) as it:
                turn(it, True, True, True)
            turn(GROUPS, False, True, True)
            turn(GROUPS + 1, False, False, True)


def kernel(**inputs):
    import numpy as np
    import concourse.bacc as bacc
    from concourse.bass_utils import run_bass_kernel_spmd

    a = {k: np.asarray(v) for k, v in inputs.items()}

    def by_channel(v):
        return v.reshape(-1, P).T

    eye = np.eye(P, dtype=np.float32)
    heads = np.kron(np.eye(HPB, dtype=np.float32), np.ones((HD, HD), np.float32))
    head = np.kron(np.eye(HPB, dtype=np.float32), np.ones((HD, 1), np.float32))
    laid = [
        ("logdt", a["L0_tok_log_dt"]),
        ("inv_ar", a["L0_tok_inv_A_real"].T),
        ("a_im", a["L0_tok_A_imag"].T),
        ("b_ri", a["L0_tok_B_ri"].transpose(2, 1, 0)),
        ("c_ri", a["x"].transpose(3, 2, 1, 0)),
        ("n1g", by_channel(a["L0_attn_norm1_g"])),
        ("n1b", by_channel(a["L0_attn_norm1_b"])),
        ("qkvT", a["L0_attn_qkv_w"].T),
        ("projT", a["L0_attn_proj_w"].T),
        ("proj_b", a["L0_attn_proj_b"]),
        ("n2g", by_channel(a["L0_attn_norm2_g"])),
        ("n2b", by_channel(a["L0_attn_norm2_b"])),
        ("fc1T", a["L0_attn_fc1_w"].T),
        ("fc1_b", by_channel(a["L0_attn_fc1_b"])),
        ("fc2T", a["L0_attn_fc2_w"].T),
        ("fc2_b", a["L0_attn_fc2_b"]),
        ("wq", a["L0_ffn_Wq"]),
        ("routersT", a["L0_ffn_routers"].T),
        ("leafT", a["L0_ffn_leaf_values"].T),
        ("woutT", a["L0_ffn_Wout_w"].T),
        ("wout_b", a["L0_ffn_Wout_b"]),
        ("consts", np.concatenate([eye, heads, head], axis=1)),
    ]
    nc = bacc.Bacc("TRN2", target_bir_lowering=False, num_devices=1)
    arrays, args = {}, []
    for name, v in laid:
        v = np.ascontiguousarray(v)
        arrays[f"in_{name}"] = v
        args.append(nc.dram_tensor(f"in_{name}", v.shape, mybir.dt.from_np(v.dtype), kind="ExternalInput").ap())
    out = nc.dram_tensor("out_tokens", (B, H, D), F32, kind="ExternalOutput").ap()
    vit_tower(nc, *args, out)
    r = run_bass_kernel_spmd(nc, [arrays], core_ids=[0])
    return r.results[0]["out_tokens"]
```
